# Optimizing a Trainium2 kernel written in Bass

```python
import numpy as np
import jax
import jax.numpy as jnp

def _softmax(x, axis=-1):
    return jax.nn.softmax(x, axis=axis)

def _gelu(x):
    return jax.nn.gelu(x, approximate=True)

def _silu(x):
    return jax.nn.silu(x)

def _sigmoid(x):
    return jax.nn.sigmoid(x)

def _layernorm(x, axis=-1, eps=1e-05):
    m = jnp.mean(x, axis=axis, keepdims=True)
    v = jnp.var(x, axis=axis, keepdims=True)
    return (x - m) / jnp.sqrt(v + eps)

def _scatter_add(tgt, idx, src, axis=0):
    return tgt.at[idx].add(src)

def _segment_sum(src, seg, n):
    return jax.ops.segment_sum(src, seg, n)
kernel_name = 'mk_cond_resid_d1_seqx_r4_5819cd'

def setup_inputs(seed: int=0):
    np.random.seed(seed)
    _w = jnp.asarray

    def _rec_inputs():
        import jax
        import jax.numpy as jnp
        _rk = jax.random.key(seed)
        x = -0.0003929 + 0.9999 * jax.random.normal(jax.random.fold_in(_rk, 1), (16, 256, 256), jnp.float32)
        _lenS = 256 - jax.random.randint(jax.random.fold_in(_rk, 7), (16,), 0, max(1, 256 // 4) + 1, jnp.int32)
        _lenS2 = 256 - jax.random.randint(jax.random.fold_in(_rk, 8), (16,), 0, max(1, 256 // 4) + 1, jnp.int32)
        itok_B_0_63 = jax.random.randint(jax.random.fold_in(_rk, 11), (16,), 0, 64, jnp.int32)
        return (x, itok_B_0_63)
    x, itok_B_0_63 = _rec_inputs()

    def _L0_cond_setup():
        import jax, jax.numpy as jnp
        import numpy as np
        NUM_CATEGORIES = 64
        INPUT_DIM = 256
        HIDDEN_DIM = 256
        B = 64
        S = 64
        key = jax.random.key(seed)
        kx, kc, kw = jax.random.split(key, 3)
        x = jax.random.normal(kx, (B, S, INPUT_DIM), dtype=jnp.float32)
        cat_ids = jax.random.randint(kc, (B,), 0, NUM_CATEGORIES, dtype=jnp.int32)
        W = 0.02 * jax.random.normal(kw, (NUM_CATEGORIES, INPUT_DIM, HIDDEN_DIM), dtype=jnp.float32)
        b = jnp.zeros((NUM_CATEGORIES, HIDDEN_DIM), dtype=jnp.float32)
        return {'x': x, 'cat_ids': cat_ids, 'W': W, 'b': b}
    _L0_cond_all = _L0_cond_setup()
    _L0_cond_in = {k: v for k, v in _L0_cond_all.items() if k in ('W', 'b')}
    del _L0_cond_all
    return {'x': x, 'itok_B_0_63': itok_B_0_63, 'L0_cond_W': _L0_cond_in['W'], 'L0_cond_b': _L0_cond_in['b']}

def reference(x, itok_B_0_63, L0_cond_W, L0_cond_b):
    import jax
    import jax.numpy as jnp

    def _L0_cond_ref(x, cat_ids, W, b):
        import jax, jax.numpy as jnp
        import numpy as np
        NUM_CATEGORIES = 64
        INPUT_DIM = 256
        HIDDEN_DIM = 256
        B = 64
        S = 64
        selected_W = W[cat_ids]
        selected_b = b[cat_ids]
        out = jnp.einsum('bsd,bdh->bsh', x, selected_W) + selected_b[:, None, :]
        return out
    x = x + _L0_cond_ref(x, itok_B_0_63, L0_cond_W, L0_cond_b)
    return x

_drawn_inputs = setup_inputs


def setup_inputs(seed=0):
    import zlib

    import numpy as np

    out = dict(_drawn_inputs(seed))
    spreads = {'L0_cond_b': (0.0, 0.1)}
    factors = {}
    for name, (base, spread) in spreads.items():
        noise = np.random.default_rng([zlib.crc32(name.encode()), seed]).standard_normal(out[name].shape)
        drawn = base * np.exp(spread * noise) if base else spread * noise
        out[name] = jnp.asarray(drawn.astype(out[name].dtype))
    for name, factor in factors.items():
        out[name] = (out[name] * factor).astype(out[name].dtype)
    return out
```

```python
from contextlib import ExitStack

import concourse.bass as bass
from concourse import mybir

P = 128


def conditional_residual_kernel(nc, x_t, ids, weights, biases, out_t):
    F32 = mybir.dt.float32
    U32 = mybir.dt.uint32
    ALU = mybir.AluOpType

    _, batches, halves, seq = x_t.shape
    categories, dim, hidden = weights.shape
    assert dim == hidden == halves * P
    PSUM_BANKS = 8
    BANK_COLUMNS = 512

    x_groups = [(0, 1), (1, 2), (2, 4), (4, 8), (8, 12), (12, 16)]
    group_of = {b: g for g, (first, end) in enumerate(x_groups) for b in range(first, end)}

    w_rows = weights.rearrange("c (p k) h -> c p (k h)", k=halves)

    with ExitStack() as ctx:
        def sb(name, shape, dt):
            return ctx.enter_context(nc.sbuf_tensor(name, shape, dt))

        def sem(name):
            return ctx.enter_context(nc.semaphore(name))

        x_sb = sb("x_sb", [P, batches, halves, seq], F32)
        w_sb = sb("w_sb", [P, batches, halves * hidden], F32)
        out_sb = sb("out_sb", [P, batches, halves, seq], F32)
        ids_col = sb("ids_col", [batches, 1], U32)
        bias_rows = sb("bias_rows", [batches, hidden], F32)
        identity = sb("identity", [batches, batches], F32)
        bias_t = sb("bias_t", [P, halves, batches], F32)

        acc = ctx.enter_context(nc.psum_tensor("acc", [P, PSUM_BANKS, BANK_COLUMNS], F32))
        bias_ps = acc[:, PSUM_BANKS - 1, 0:halves * batches].rearrange("p (m b) -> p m b", m=halves)

        x_landed = [sem(f"x_landed{g}") for g in range(len(x_groups))]
        w_landed = [sem(f"w_landed{b}") for b in range(batches)]
        ids_landed = sem("ids_landed")
        bias_rows_landed = sem("bias_rows_landed")
        identity_zeroed = sem("identity_zeroed")
        identity_ready = sem("identity_ready")
        bias_transposed = sem("bias_transposed")
        bias_ready = sem("bias_ready")
        product_ready = sem("product_ready")
        sum_ready = sem("sum_ready")
        out_stored = sem("out_stored")

        block = ctx.enter_context(nc.Block())

        @block.sync
        def _(sp):
            for g, (first, end) in enumerate(x_groups):
                sp.dma_start(x_sb[:, first:end], x_t[:, first:end]).then_inc(x_landed[g], 16)
            for b in range(batches):
                sp.wait_ge(sum_ready, halves * (b + 1))
                sp.dma_start(out_t[:, b], out_sb[:, b]).then_inc(out_stored, 16)
            sp.wait_ge(out_stored, 16 * batches)

        @block.scalar
        def _(act):
            for b in range(batches):
                category = act.value_load(ids[0:1, b:b + 1], min_val=0, max_val=categories - 1)
                act.dma_start(w_sb[:, b, :], w_rows[bass.ds(category, 1), :, :].rearrange("c p n -> (c p) n")
                              ).then_inc(w_landed[b], 16)

        @block.gpsimd
        def _(pool):
            pool.dma_start(ids_col[:, :], ids.rearrange("a b -> b a").bitcast(U32)).then_inc(ids_landed, 16)
            pool.memset(identity[:, :], 0.0).then_inc(identity_zeroed, 1)
            pool.wait_ge(identity_zeroed, 1)
            pool.affine_select(out=identity[:, :], in_=identity[:, :], compare_op=ALU.not_equal, fill=1.0,
                               base=0, pattern=[[-1, batches]], channel_multiplier=1).then_inc(identity_ready, 1)
            pool.wait_ge(ids_landed, 16)
            pool.indirect_dma_start(bias_rows[:, :], None, biases[:, :],
                                    bass.IndirectOffsetOnAxis(ap=ids_col[:, 0:1], axis=0)
                                    ).then_inc(bias_rows_landed, 16)

        @block.tensor
        def _(pe):
            pe.wait_ge(identity_ready, 1)
            pe.wait_ge(bias_rows_landed, 16)
            bias_cols = bias_rows[:, :].rearrange("b (p m) -> b m p", m=halves)
            for m in range(halves):
                last = nc.tensor.transpose(bias_ps[:, m, :], bias_cols[:, m, :], identity[:, :])
            last.then_inc(bias_transposed, 1)
            for b in range(batches):
                pe.wait_ge(x_landed[group_of[b]], 16)
                pe.wait_ge(w_landed[b], 16)
                w = w_sb[:, b, :].rearrange("p (k q m) -> p k m q", k=halves, m=halves)
                for m in range(halves):
                    unit = halves * b + m
                    if unit == PSUM_BANKS - 1:
                        pe.wait_ge(bias_ready, 1)
                    if unit >= PSUM_BANKS:
                        pe.wait_ge(sum_ready, unit - PSUM_BANKS + 1)
                    for k in range(halves):
                        last = nc.tensor.matmul(acc[:, unit % PSUM_BANKS, 0:seq], w[:, k, m, :], x_sb[:, b, k, :],
                                                start=(k == 0), stop=(k == halves - 1))
                    last.then_inc(product_ready, 1)

        @block.vector
        def _(dve):
            dve.wait_ge(bias_transposed, 1)
            nc.vector.tensor_copy(bias_t[:, :, :], bias_ps).then_inc(bias_ready, 1)
            dve.wait_ge(bias_ready, 1)
            for b in range(batches):
                dve.wait_ge(x_landed[group_of[b]], 16)
                for m in range(halves):
                    unit = halves * b + m
                    dve.wait_ge(product_ready, unit + 1)
                    nc.vector.scalar_tensor_tensor(out=out_sb[:, b, m, :], in0=acc[:, unit % PSUM_BANKS, 0:seq],
                                                   scalar=bias_t[:, m, b:b + 1], in1=x_sb[:, b, m, :],
                                                   op0=ALU.add, op1=ALU.add).then_inc(sum_ready, 1)


def kernel(x, itok_B_0_63, L0_cond_W, L0_cond_b):
    import numpy as np
    import concourse.bacc as bacc
    from concourse.bass_utils import run_bass_kernel_spmd

    x = np.asarray(x)
    batches, seq, dim = x.shape
    halves = dim // P
    arrays = {
        "x_t": np.ascontiguousarray(x.reshape(batches, seq, P, halves).transpose(2, 0, 3, 1)),
        "ids": np.ascontiguousarray(itok_B_0_63).reshape(1, batches),
        "weights": np.ascontiguousarray(L0_cond_W),
        "biases": np.ascontiguousarray(L0_cond_b),
    }
    nc = bacc.Bacc("TRN2", target_bir_lowering=False, num_devices=1)
    ins = [nc.dram_tensor(n, a.shape, mybir.dt.from_np(a.dtype), kind="ExternalInput").ap()
           for n, a in arrays.items()]
    out = nc.dram_tensor("out_t", arrays["x_t"].shape, mybir.dt.float32, kind="ExternalOutput").ap()
    conditional_residual_kernel(nc, *ins, out)
    result = run_bass_kernel_spmd(nc, [arrays], core_ids=[0]).results[0]["out_t"]
    return np.ascontiguousarray(result.transpose(1, 3, 0, 2)).reshape(batches, seq, dim)
```

```python
from contextlib import ExitStack

import concourse.bass as bass
from concourse import mybir

P = 128
PSUM_BANKS = 8
BANK_COLUMNS = 512
WARM_UP_MATMULS = 9
IDS_PER_FETCH = 4
STORE_BATCHES = 2


def conditional_residual_kernel(nc, x_t, ids, weights, biases_t, out_t):
    F32 = mybir.dt.float32
    BF16 = mybir.dt.bfloat16
    ALU = mybir.AluOpType

    _, batches, halves, seq = x_t.shape
    categories, dim, hidden = weights.shape
    assert dim == hidden == halves * P and seq <= BANK_COLUMNS

    x_groups = [(0, 1), (1, 2)] + [(b, b + 2) for b in range(2, batches, 2)]
    group_of = {b: g for g, (first, end) in enumerate(x_groups) for b in range(first, end)}
    round_batches = PSUM_BANKS // halves
    assert batches % STORE_BATCHES == 0 and batches % round_batches == 0

    w_rows = weights.rearrange("c (p k) h -> c p (k h)", k=halves)

    with ExitStack() as ctx:
        def sb(name, shape, dt):
            return ctx.enter_context(nc.sbuf_tensor(name, shape, dt))

        def sem(name):
            return ctx.enter_context(nc.semaphore(name))

        x_sb = sb("x_sb", [P, batches, halves, seq], F32)
        w_sb = sb("w_sb", [P, batches, halves * hidden], F32)
        out_sb = sb("out_sb", [P, batches, halves, seq], F32)
        bias_t = sb("bias_t", [P, categories, halves], F32)
        zeros = sb("zeros", [P, BANK_COLUMNS], BF16)

        acc = ctx.enter_context(nc.psum_tensor("acc", [P, PSUM_BANKS, BANK_COLUMNS], F32))
        warm_up_ps = acc[:, PSUM_BANKS - 1, :]

        x_landed = [sem(f"x_landed{g}") for g in range(len(x_groups))]
        w_landed = [sem(f"w_landed{b}") for b in range(batches)]
        biases_landed = sem("biases_landed")
        zeros_ready = sem("zeros_ready")
        product_ready = sem("product_ready")
        sum_ready = sem("sum_ready")
        out_stored = sem("out_stored")

        def load_categories(engine, first, count):
            _, values = nc.values_load_multi_w_load_instructions(
                ids[0:1, bass.ds(first, count)], engines=[engine.engine], min_val=0, max_val=categories - 1,
                skip_runtime_bounds_check_because="an id is a category number, so 0 <= id < categories")
            return list(values)

        def load_x(engine, g):
            first, end = x_groups[g]
            engine.dma_start(x_sb[:, first:end], x_t[:, first:end]).then_inc(x_landed[g], 16)

        block = ctx.enter_context(nc.Block())

        @block.sync
        def _(sp):
            load_x(sp, 0)
            load_x(sp, 1)
            sp.dma_start(bias_t[:, :, :], biases_t).then_inc(biases_landed, 16)
            paired_stores = batches // STORE_BATCHES - 1
            with sp.Fori(0, paired_stores) as i:
                group = bass.ds(i * STORE_BATCHES, STORE_BATCHES)
                sp.wait_ge(sum_ready, (i + 1) * (STORE_BATCHES * halves))
                sp.dma_start(out_t[:, group], out_sb[:, group]).then_inc(out_stored, 16)
            last_batch = batches - 1
            for b in range(paired_stores * STORE_BATCHES, last_batch):
                sp.wait_ge(sum_ready, halves * (b + 1))
                sp.dma_start(out_t[:, b], out_sb[:, b]).then_inc(out_stored, 16)
            for m in range(halves):
                sp.wait_ge(sum_ready, halves * last_batch + m + 1)
                sp.dma_start(out_t[:, last_batch, m], out_sb[:, last_batch, m]).then_inc(out_stored, 16)
            sp.wait_ge(out_stored, 16 * (paired_stores + STORE_BATCHES - 1 + halves))

        @block.scalar
        def _(act):
            def load_w(b, category):
                act.dma_start(w_sb[:, b, :], w_rows[bass.ds(category, 1), :, :].rearrange("c p n -> (c p) n")
                              ).then_inc(w_landed[b], 16)

            loaded_group = 1
            for b in range(batches):
                if b % IDS_PER_FETCH == 0:
                    categories_of = load_categories(act, b, IDS_PER_FETCH)
                load_w(b, categories_of[b % IDS_PER_FETCH])
                if b + 1 < batches and group_of[b + 1] > loaded_group:
                    loaded_group += 1
                    load_x(act, loaded_group)

        @block.tensor
        def _(pe):
            pe.wait_ge(zeros_ready, 1)
            for _ in range(WARM_UP_MATMULS):
                nc.tensor.matmul(warm_up_ps, zeros[:, 0:P], zeros[:, :], start=True, stop=True)

            for b in range(batches):
                pe.wait_ge(x_landed[group_of[b]], 16)
                pe.wait_ge(w_landed[b], 16)
                w = w_sb[:, b, :].rearrange("p (k q m) -> p k m q", k=halves, m=halves)
                for m in range(halves):
                    unit = halves * b + m
                    if unit >= PSUM_BANKS:
                        pe.wait_ge(sum_ready, unit - PSUM_BANKS + 1)
                    for k in range(halves):
                        last = nc.tensor.matmul(acc[:, unit % PSUM_BANKS, 0:seq], w[:, k, m, :], x_sb[:, b, k, :],
                                                start=(k == 0), stop=(k == halves - 1))
                    last.then_inc(product_ready, 1)

        @block.vector
        def _(dve):
            dve.memset(zeros[:, :], 0.0).then_inc(zeros_ready, 1)
            dve.wait_ge(biases_landed, 16)
            with dve.Fori(0, batches // round_batches) as i:
                categories_of = load_categories(dve, i * round_batches, round_batches)
                for j in range(round_batches):
                    b = bass.ds(i * round_batches + j, 1)
                    for m in range(halves):
                        bank = halves * j + m
                        dve.wait_ge(product_ready, i * PSUM_BANKS + (bank + 1))
                        dve.scalar_tensor_tensor(out=out_sb[:, b, m, :], in0=acc[:, bank, 0:seq],
                                                 scalar=bias_t[:, bass.ds(categories_of[j], 1), m],
                                                 in1=x_sb[:, b, m, :], op0=ALU.add, op1=ALU.add
                                                 ).then_inc(sum_ready, 1)


def kernel(x, itok_B_0_63, L0_cond_W, L0_cond_b):
    import numpy as np
    import concourse.bacc as bacc
    from concourse.bass_utils import run_bass_kernel_spmd

    x = np.asarray(x)
    batches, seq, dim = x.shape
    halves = dim // P
    arrays = {
        "x_t": np.ascontiguousarray(x.reshape(batches, seq, P, halves).transpose(2, 0, 3, 1)),
        "ids": np.ascontiguousarray(itok_B_0_63).reshape(1, batches),
        "weights": np.ascontiguousarray(L0_cond_W),
        "biases_t": np.ascontiguousarray(np.asarray(L0_cond_b).reshape(-1, P, halves).transpose(1, 0, 2)),
    }
    nc = bacc.Bacc("TRN2", target_bir_lowering=False, num_devices=1)
    ins = [nc.dram_tensor(name, a.shape, mybir.dt.from_np(a.dtype), kind="ExternalInput").ap()
           for name, a in arrays.items()]
    out = nc.dram_tensor("out_t", arrays["x_t"].shape, mybir.dt.float32, kind="ExternalOutput").ap()
    conditional_residual_kernel(nc, *ins, out)
    result = run_bass_kernel_spmd(nc, [arrays], core_ids=[0]).results[0]["out_t"]
    return np.ascontiguousarray(result.transpose(1, 3, 0, 2)).reshape(batches, seq, dim)
```
